# Optimizing a Trainium2 kernel written in Bass

```python
import numpy as np
import jax
import jax.numpy as jnp

def _softmax(x, axis=-1):
    return jax.nn.softmax(x, axis=axis)

def _gelu(x):
    return jax.nn.gelu(x, approximate=True)

def _silu(x):
    return jax.nn.silu(x)

def _sigmoid(x):
    return jax.nn.sigmoid(x)

def _layernorm(x, axis=-1, eps=1e-05):
    m = jnp.mean(x, axis=axis, keepdims=True)
    v = jnp.var(x, axis=axis, keepdims=True)
    return (x - m) / jnp.sqrt(v + eps)

def _scatter_add(tgt, idx, src, axis=0):
    return tgt.at[idx].add(src)

def _segment_sum(src, seg, n):
    return jax.ops.segment_sum(src, seg, n)
kernel_name = 'mk_gnn_preln_d4_gnn_r16_d4c8c2'

def setup_inputs(seed: int=0):
    np.random.seed(seed)
    _w = jnp.asarray

    def _rec_inputs():
        import jax
        import jax.numpy as jnp
        _gk = jax.random.key(seed)
        x = -0.0003713 + 1 * jax.random.normal(jax.random.fold_in(_gk, 1), (6250, 128), jnp.float32)
        src = jax.random.randint(jax.random.fold_in(_gk, 2), (100000,), 0, 6250, jnp.int32)
        dst = jnp.minimum((6250 * jax.random.uniform(jax.random.fold_in(_gk, 3), (100000,)) ** 2.0).astype(jnp.int32), 99999)
        _o = jnp.argsort(dst, stable=True)
        src = src[_o]
        dst = dst[_o]
        return (x, src, dst)
    x, src, dst = _rec_inputs()

    def _L0_gnn_setup():
        import jax, jax.numpy as jnp
        import numpy as np
        N, E = (6250, 100000)
        NFEAT, NHID, HEADS = (128, 128, 2)
        FOUT = NHID // 2
        NEG_SLOPE = 0.2
        LN_EPS = 1e-05
        key = jax.random.key(seed)
        ks = jax.random.split(key, 10)
        h = jax.random.normal(ks[0], (N, NFEAT), dtype=jnp.float32)
        src = jax.random.randint(ks[1], (E,), 0, N, dtype=jnp.int32)
        dst = jax.random.randint(ks[2], (E,), 0, N, dtype=jnp.int32)
        W = jax.random.normal(ks[3], (NFEAT, HEADS * FOUT), dtype=jnp.float32) / np.sqrt(NFEAT)
        attn_l = jax.random.normal(ks[4], (HEADS, FOUT), dtype=jnp.float32) * 0.1
        attn_r = jax.random.normal(ks[5], (HEADS, FOUT), dtype=jnp.float32) * 0.1
        bias = jnp.zeros((HEADS * FOUT,), dtype=jnp.float32)
        gamma = jnp.ones((NHID,), dtype=jnp.float32)
        beta = jnp.zeros((NHID,), dtype=jnp.float32)
        return {'h': h, 'src': src, 'dst': dst, 'W': W, 'attn_l': attn_l, 'attn_r': attn_r, 'bias': bias, 'gamma': gamma, 'beta': beta}
    _L0_gnn_all = _L0_gnn_setup()
    _L0_gnn_in = {k: v for k, v in _L0_gnn_all.items() if k in ('W', 'attn_l', 'attn_r', 'bias', 'gamma', 'beta')}
    del _L0_gnn_all

    def _L1_gnn_setup():
        import jax, jax.numpy as jnp
        import numpy as np
        N = 3125
        E = 50000
        IN_DIM = 128
        HID = 64
        HEADS = 4
        OUT_DIM = 128

        def _gat_conv(x, src, dst, W, a_src, a_dst, bias, heads, out_ch):
            n = x.shape[0]
            h = (x @ W).reshape(n, heads, out_ch)
            alpha_s = jnp.einsum('nhc,hc->nh', h, a_src)
            alpha_d = jnp.einsum('nhc,hc->nh', h, a_dst)
            e = jax.nn.leaky_relu(alpha_s[src] + alpha_d[dst], 0.2)
            m = jax.ops.segment_max(e, dst, num_segments=n)
            m = jnp.where(jnp.isfinite(m), m, 0.0)
            ex = jnp.exp(e - m[dst])
            denom = jax.ops.segment_sum(ex, dst, num_segments=n)
            alpha = ex / denom[dst]
            out = jax.ops.segment_sum(alpha[:, :, None] * h[src], dst, num_segments=n)
            return out.reshape(n, heads * out_ch) + bias
        key = jax.random.key(seed)
        ks = jax.random.split(key, 12)
        s = lambda fan: 1.0 / np.sqrt(fan)
        return {'features': jax.random.normal(ks[0], (N, IN_DIM), jnp.float32), 'edge_index': jax.random.randint(ks[1], (2, E), 0, N, jnp.int64), 'W1': jax.random.normal(ks[2], (IN_DIM, HEADS * HID), jnp.float32) * s(IN_DIM), 'att_src1': jax.random.normal(ks[3], (HEADS, HID), jnp.float32) * s(HID), 'att_dst1': jax.random.normal(ks[4], (HEADS, HID), jnp.float32) * s(HID), 'bias1': jnp.zeros((HEADS * HID,), jnp.float32), 'W2': jax.random.normal(ks[5], (HEADS * HID, OUT_DIM), jnp.float32) * s(HEADS * HID), 'att_src2': jax.random.normal(ks[6], (1, OUT_DIM), jnp.float32) * s(OUT_DIM), 'att_dst2': jax.random.normal(ks[7], (1, OUT_DIM), jnp.float32) * s(OUT_DIM), 'bias2': jnp.zeros((OUT_DIM,), jnp.float32)}
    _L1_gnn_all = _L1_gnn_setup()
    _L1_gnn_in = {k: v for k, v in _L1_gnn_all.items() if k in ('W1', 'att_src1', 'att_dst1', 'bias1', 'W2', 'att_src2', 'att_dst2', 'bias2')}
    del _L1_gnn_all

    def _L2_gnn_setup():
        import jax, jax.numpy as jnp
        import numpy as np
        N = 6250
        E = 100000
        D_IN = 128
        D_HID = 128
        D_OUT = 128

        def _sage_conv(h, src, dst, Wl, bl, Wr):
            msgs = h[src]
            agg = jax.ops.segment_sum(msgs, dst, num_segments=N)
            deg = jax.ops.segment_sum(jnp.ones((src.shape[0],), h.dtype), dst, num_segments=N)
            agg = agg / jnp.maximum(deg, 1.0)[:, None]
            return agg @ Wl.T + bl + h @ Wr.T
        key = jax.random.key(seed)
        ks = jax.random.split(key, 8)
        x = jax.random.normal(ks[0], (N, D_IN), dtype=jnp.float32)
        edge_index = jax.random.randint(ks[1], (2, E), 0, N, dtype=jnp.int64)
        s = 0.02
        W1l = jax.random.normal(ks[2], (D_HID, D_IN), dtype=jnp.float32) * s
        b1l = jnp.zeros((D_HID,), dtype=jnp.float32)
        W1r = jax.random.normal(ks[3], (D_HID, D_IN), dtype=jnp.float32) * s
        W2l = jax.random.normal(ks[4], (D_OUT, D_HID), dtype=jnp.float32) * s
        b2l = jnp.zeros((D_OUT,), dtype=jnp.float32)
        W2r = jax.random.normal(ks[5], (D_OUT, D_HID), dtype=jnp.float32) * s
        return {'x': x, 'edge_index': edge_index, 'W1l': W1l, 'b1l': b1l, 'W1r': W1r, 'W2l': W2l, 'b2l': b2l, 'W2r': W2r}
    _L2_gnn_all = _L2_gnn_setup()
    _L2_gnn_in = {k: v for k, v in _L2_gnn_all.items() if k in ('W1l', 'b1l', 'W1r', 'W2l', 'b2l', 'W2r')}
    del _L2_gnn_all

    def _L3_gnn_setup():
        import jax, jax.numpy as jnp
        import numpy as np
        H = 2
        C = 128
        K_ORDER = 4
        BETA = 0.5

        def _gcn_conv(x, row, col, deg_inv, n):
            msg = x[row]
            agg = jax.ops.segment_sum(msg, col, num_segments=n)
            return agg * deg_inv[:, None, None]

        def _attn_conv(qs, ks, vs):
            n = qs.shape[0]
            kvs = jnp.einsum('lhm,lhd->hmd', ks, vs)
            qkvs = jnp.einsum('nhm,hmd->nhd', qs, kvs)
            vs_sum = vs.sum(axis=0)
            num = qkvs + vs_sum[None, :, :]
            ks_sum = ks.sum(axis=0)
            qks_sum = jnp.einsum('nhm,hm->nh', qs, ks_sum)[:, :, None]
            den = qks_sum + jnp.asarray(n, qs.dtype)
            return num / den
        key = jax.random.key(seed)
        ks = jax.random.split(key, 8)
        N, E = (6250, 100000)
        x = jax.random.normal(ks[0], (N, C), jnp.float32)
        edge_index = jax.random.randint(ks[1], (2, E), 0, N, jnp.int64)
        s_in = 1.0 / np.sqrt(C)
        s_out = 1.0 / np.sqrt(H * C * (K_ORDER + 1))
        Wq_w = jax.random.normal(ks[2], (C, H * C), jnp.float32) * s_in
        Wq_b = jax.random.normal(ks[3], (H * C,), jnp.float32) * s_in
        Wk_w = jax.random.normal(ks[4], (C, H * C), jnp.float32) * s_in
        Wk_b = jax.random.normal(ks[5], (H * C,), jnp.float32) * s_in
        Wo_w = jax.random.normal(ks[6], (H * C * (K_ORDER + 1), C), jnp.float32) * s_out
        Wo_b = jax.random.normal(ks[7], (C,), jnp.float32) * s_out
        return {'x': x, 'edge_index': edge_index, 'Wq_w': Wq_w, 'Wq_b': Wq_b, 'Wk_w': Wk_w, 'Wk_b': Wk_b, 'Wo_w': Wo_w, 'Wo_b': Wo_b}
    _L3_gnn_all = _L3_gnn_setup()
    _L3_gnn_in = {k: v for k, v in _L3_gnn_all.items() if k in ('Wq_w', 'Wq_b', 'Wk_w', 'Wk_b', 'Wo_w', 'Wo_b')}
    del _L3_gnn_all
    return {'x': x, 'src': src, 'dst': dst, 'L0_gnn_W': _L0_gnn_in['W'], 'L0_gnn_attn_l': _L0_gnn_in['attn_l'], 'L0_gnn_attn_r': _L0_gnn_in['attn_r'], 'L0_gnn_bias': _L0_gnn_in['bias'], 'L0_gnn_gamma': _L0_gnn_in['gamma'], 'L0_gnn_beta': _L0_gnn_in['beta'], 'L1_gnn_W1': _L1_gnn_in['W1'], 'L1_gnn_att_src1': _L1_gnn_in['att_src1'], 'L1_gnn_att_dst1': _L1_gnn_in['att_dst1'], 'L1_gnn_bias1': _L1_gnn_in['bias1'], 'L1_gnn_W2': _L1_gnn_in['W2'], 'L1_gnn_att_src2': _L1_gnn_in['att_src2'], 'L1_gnn_att_dst2': _L1_gnn_in['att_dst2'], 'L1_gnn_bias2': _L1_gnn_in['bias2'], 'L2_gnn_W1l': _L2_gnn_in['W1l'], 'L2_gnn_b1l': _L2_gnn_in['b1l'], 'L2_gnn_W1r': _L2_gnn_in['W1r'], 'L2_gnn_W2l': _L2_gnn_in['W2l'], 'L2_gnn_b2l': _L2_gnn_in['b2l'], 'L2_gnn_W2r': _L2_gnn_in['W2r'], 'L3_gnn_Wq_w': _L3_gnn_in['Wq_w'], 'L3_gnn_Wq_b': _L3_gnn_in['Wq_b'], 'L3_gnn_Wk_w': _L3_gnn_in['Wk_w'], 'L3_gnn_Wk_b': _L3_gnn_in['Wk_b'], 'L3_gnn_Wo_w': _L3_gnn_in['Wo_w'], 'L3_gnn_Wo_b': _L3_gnn_in['Wo_b']}

def reference(x, src, dst, L0_gnn_W, L0_gnn_attn_l, L0_gnn_attn_r, L0_gnn_bias, L0_gnn_gamma, L0_gnn_beta, L1_gnn_W1, L1_gnn_att_src1, L1_gnn_att_dst1, L1_gnn_bias1, L1_gnn_W2, L1_gnn_att_src2, L1_gnn_att_dst2, L1_gnn_bias2, L2_gnn_W1l, L2_gnn_b1l, L2_gnn_W1r, L2_gnn_W2l, L2_gnn_b2l, L2_gnn_W2r, L3_gnn_Wq_w, L3_gnn_Wq_b, L3_gnn_Wk_w, L3_gnn_Wk_b, L3_gnn_Wo_w, L3_gnn_Wo_b):
    import jax
    import jax.numpy as jnp

    def _L0_gnn_ref(h, src, dst, W, attn_l, attn_r, bias, gamma, beta):
        import jax, jax.numpy as jnp
        import numpy as np
        N, E = (6250, 100000)
        NFEAT, NHID, HEADS = (128, 128, 2)
        FOUT = NHID // 2
        NEG_SLOPE = 0.2
        LN_EPS = 1e-05
        feat = (h @ W).reshape(N, HEADS, FOUT)
        el = jnp.einsum('nhf,hf->nh', feat, attn_l)
        er = jnp.einsum('nhf,hf->nh', feat, attn_r)
        e = jax.nn.leaky_relu(el[src] + er[dst], NEG_SLOPE)
        emax = jax.ops.segment_max(e, dst, num_segments=N)
        expe = jnp.exp(e - emax[dst])
        denom = jax.ops.segment_sum(expe, dst, num_segments=N)
        alpha = expe / denom[dst]
        msg = feat[src] * alpha[:, :, None]
        out = jax.ops.segment_sum(msg, dst, num_segments=N)
        x = out.reshape(N, HEADS * FOUT) + bias
        mu = jnp.mean(x, axis=-1, keepdims=True)
        var = jnp.mean(jnp.square(x - mu), axis=-1, keepdims=True)
        return gamma * (x - mu) * jax.lax.rsqrt(var + LN_EPS) + beta

    def _L1_gnn_ref(features, edge_index, W1, att_src1, att_dst1, bias1, W2, att_src2, att_dst2, bias2):
        import jax, jax.numpy as jnp
        import numpy as np
        N = 3125
        E = 50000
        IN_DIM = 128
        HID = 64
        HEADS = 4
        OUT_DIM = 128

        def _gat_conv(x, src, dst, W, a_src, a_dst, bias, heads, out_ch):
            n = x.shape[0]
            h = (x @ W).reshape(n, heads, out_ch)
            alpha_s = jnp.einsum('nhc,hc->nh', h, a_src)
            alpha_d = jnp.einsum('nhc,hc->nh', h, a_dst)
            e = jax.nn.leaky_relu(alpha_s[src] + alpha_d[dst], 0.2)
            m = jax.ops.segment_max(e, dst, num_segments=n)
            m = jnp.where(jnp.isfinite(m), m, 0.0)
            ex = jnp.exp(e - m[dst])
            denom = jax.ops.segment_sum(ex, dst, num_segments=n)
            alpha = ex / denom[dst]
            out = jax.ops.segment_sum(alpha[:, :, None] * h[src], dst, num_segments=n)
            return out.reshape(n, heads * out_ch) + bias
        n = features.shape[0]
        loops = jnp.arange(n, dtype=edge_index.dtype)
        src = jnp.concatenate([edge_index[0], loops])
        dst = jnp.concatenate([edge_index[1], loops])
        act = lambda v: jax.nn.leaky_relu(v, 0.2)
        x = _gat_conv(features, src, dst, W1, att_src1, att_dst1, bias1, HEADS, HID)
        x = act(x)
        x = _gat_conv(x, src, dst, W2, att_src2, att_dst2, bias2, 1, OUT_DIM)
        x = act(x)
        return x + features

    def _L2_gnn_ref(x, edge_index, W1l, b1l, W1r, W2l, b2l, W2r):
        import jax, jax.numpy as jnp
        import numpy as np
        N = 6250
        E = 100000
        D_IN = 128
        D_HID = 128
        D_OUT = 128

        def _sage_conv(h, src, dst, Wl, bl, Wr):
            msgs = h[src]
            agg = jax.ops.segment_sum(msgs, dst, num_segments=N)
            deg = jax.ops.segment_sum(jnp.ones((src.shape[0],), h.dtype), dst, num_segments=N)
            agg = agg / jnp.maximum(deg, 1.0)[:, None]
            return agg @ Wl.T + bl + h @ Wr.T
        src, dst = (edge_index[0], edge_index[1])
        h = jax.nn.relu(_sage_conv(x, src, dst, W1l, b1l, W1r))
        return _sage_conv(h, src, dst, W2l, b2l, W2r)

    def _L3_gnn_ref(x, edge_index, Wq_w, Wq_b, Wk_w, Wk_b, Wo_w, Wo_b):
        import jax, jax.numpy as jnp
        import numpy as np
        H = 2
        C = 128
        K_ORDER = 4
        BETA = 0.5

        def _gcn_conv(x, row, col, deg_inv, n):
            msg = x[row]
            agg = jax.ops.segment_sum(msg, col, num_segments=n)
            return agg * deg_inv[:, None, None]

        def _attn_conv(qs, ks, vs):
            n = qs.shape[0]
            kvs = jnp.einsum('lhm,lhd->hmd', ks, vs)
            qkvs = jnp.einsum('nhm,hmd->nhd', qs, kvs)
            vs_sum = vs.sum(axis=0)
            num = qkvs + vs_sum[None, :, :]
            ks_sum = ks.sum(axis=0)
            qks_sum = jnp.einsum('nhm,hm->nh', qs, ks_sum)[:, :, None]
            den = qks_sum + jnp.asarray(n, qs.dtype)
            return num / den
        n = x.shape[0]
        row, col = (edge_index[0], edge_index[1])
        deg = jax.ops.segment_sum(jnp.ones(row.shape[0], x.dtype), col, num_segments=n)
        deg_inv = jnp.where(deg > 0, 1.0 / deg, 0.0)
        query = (x @ Wq_w + Wq_b).reshape(n, H, C)
        key = (x @ Wk_w + Wk_b).reshape(n, H, C)
        qs = query / jnp.linalg.norm(query, axis=2, keepdims=True)
        ks = key / jnp.linalg.norm(key, axis=2, keepdims=True)
        x0 = jnp.broadcast_to(x[:, None, :], (n, H, C))
        terms = [x0]
        for _ in range(K_ORDER):
            prev = terms[-1]
            gcn_i = _gcn_conv(prev, row, col, deg_inv, n)
            attn_i = _attn_conv(qs, ks, prev)
            terms.append(BETA * gcn_i + attn_i)
        xcat = jnp.concatenate(terms, axis=-1)
        xcat = xcat.reshape(n, H * C * (K_ORDER + 1))
        return (xcat @ Wo_w + Wo_b) / H
    edge_index = jnp.stack([src, dst])
    h = jnp.maximum(_layernorm(x, axis=-1), 0.0)
    x = x + _L0_gnn_ref(h, src, dst, L0_gnn_W, L0_gnn_attn_l, L0_gnn_attn_r, L0_gnn_bias, L0_gnn_gamma, L0_gnn_beta)
    h = jnp.maximum(_layernorm(x, axis=-1), 0.0)
    x = x + _L1_gnn_ref(h, edge_index, L1_gnn_W1, L1_gnn_att_src1, L1_gnn_att_dst1, L1_gnn_bias1, L1_gnn_W2, L1_gnn_att_src2, L1_gnn_att_dst2, L1_gnn_bias2)
    h = jnp.maximum(_layernorm(x, axis=-1), 0.0)
    x = x + _L2_gnn_ref(h, edge_index, L2_gnn_W1l, L2_gnn_b1l, L2_gnn_W1r, L2_gnn_W2l, L2_gnn_b2l, L2_gnn_W2r)
    h = jnp.maximum(_layernorm(x, axis=-1), 0.0)
    x = x + _L3_gnn_ref(h, edge_index, L3_gnn_Wq_w, L3_gnn_Wq_b, L3_gnn_Wk_w, L3_gnn_Wk_b, L3_gnn_Wo_w, L3_gnn_Wo_b)
    return x

_drawn_inputs = setup_inputs


def setup_inputs(seed=0):
    import zlib

    import numpy as np

    out = dict(_drawn_inputs(seed))
    spreads = {'L0_gnn_bias': (0.0, 0.1),
     'L0_gnn_gamma': (1.0, 0.2),
     'L0_gnn_beta': (0.0, 0.1),
     'L1_gnn_bias1': (0.0, 0.347),
     'L1_gnn_bias2': (0.0, 0.1),
     'L2_gnn_b1l': (0.0, 0.682),
     'L2_gnn_b2l': (0.0, 0.1)}
    factors = {'L1_gnn_att_src1': 8.0,
     'L1_gnn_att_dst1': 172.002,
     'L1_gnn_att_src2': 36.014,
     'L1_gnn_att_dst2': 200.0,
     'L2_gnn_W1l': 3.811,
     'L2_gnn_W1r': 3.526,
     'L3_gnn_Wq_w': 200.0,
     'L3_gnn_Wq_b': 200.0,
     'L3_gnn_Wk_w': 200.0,
     'L3_gnn_Wk_b': 200.0,
     'L3_gnn_Wo_b': 8.0}
    for name, (base, spread) in spreads.items():
        noise = np.random.default_rng([zlib.crc32(name.encode()), seed]).standard_normal(out[name].shape)
        drawn = base * np.exp(spread * noise) if base else spread * noise
        out[name] = jnp.asarray(drawn.astype(out[name].dtype))
    for name, factor in factors.items():
        out[name] = (out[name] * factor).astype(out[name].dtype)
    return out
```

```python
import numpy as np
import concourse.bass as bass
from concourse import mybir

F32 = mybir.dt.float32
BF16 = mybir.dt.bfloat16
I32 = mybir.dt.int32
U32 = mybir.dt.uint32
I16 = mybir.dt.int16
ALU = mybir.AluOpType
ACT = mybir.ActivationFunctionType
AX = mybir.AxisListType.X
ds = bass.ds

P = 128
N = 6250
E = 100000
D = 128
NBLK = -(-N // P)
NPAD = NBLK * P
TAIL_NODES = N - (NBLK - 1) * P
ROWT = 7
ROWE = ROWT * P
ROWS = -(-E // ROWE)
NT = ROWS * ROWT
EPAD = NT * P
LAST_TILE = E // P
FULL_ROWS = E // ROWE
TAIL = E - FULL_ROWS * ROWE
RING = 16
HALF = RING // 2
CHUNK = 16
NCHUNK = NT // CHUNK
GCOLS = 392
NEG = -1.0e38
EPS = 1e-5
SLOPE = 0.2
BIG_INDEX = 1 << 20
OH_MATS = 48
assert NT % RING == 0 and NT % CHUNK == 0 and E % P == 32 and GCOLS == 8 * NBLK


class Signal:

    def __init__(self, nc, name):
        self.sem = nc.alloc_semaphore(name)
        self.past = 0

    def ended(self, n):
        self.past += n


class Carve:

    def __init__(self, ap):
        self.ap = ap
        self.at = 0

    def take(self, shape, dt=F32):
        n = int(np.prod(shape))
        words = n if dt in (F32, I32, U32) else -(-n // 2)
        words += words % 2
        v = self.ap[:, self.at:self.at + words]
        self.at += words
        assert self.at <= self.ap.shape[1], (self.at, self.ap.shape)
        if dt != F32:
            v = v.bitcast(dt)
        v = v[:, 0:n]
        if len(shape) == 2:
            v = v.rearrange("p (a b) -> p a b", b=shape[1])
        elif len(shape) == 3:
            v = v.rearrange("p (a b c) -> p a b c", b=shape[1], c=shape[2])
        return v


class Mem:
    pass


def allocate(nc):
    m = Mem()

    def sb(name, free, dt=F32):
        return nc.alloc_sbuf_tensor(name, [P, free], dt)[:, :]

    m.x = sb("x_res", NBLK * D).rearrange("p (b d) -> p b d", d=D)
    m.h = sb("h_norm", NBLK * D).rearrange("p (b d) -> p b d", d=D)
    m.src_idx = sb("src_idx", NT, U32)
    m.dst_f = sb("dst_f", NT)
    m.src_hi = sb("src_hi", NT, BF16)
    m.iota_n = sb("iota_n", NPAD, I16)
    m.iota_p = sb("iota_p", 2)
    m.iota_c = sb("iota_c", P, BF16)
    m.ident = sb("ident", P)
    m.ident_b = sb("ident_b", P, BF16)
    m.ones = sb("ones", P)
    m.zero = sb("zero", 512, BF16)
    m.mask = sb("mask", NBLK)
    m.deg = sb("deg", NBLK)
    m.deg_inv = sb("deg_inv", NBLK)
    m.has = sb("has", NBLK)
    m.first_tile = sb("first_tile", 64, I32)
    m.idx_stage = sb("idx_stage", RING, U32)
    m.start_idx = sb("start_idx", NBLK, U32)
    m.last_idx = sb("last_idx", NBLK, U32)
    m.seg_start = sb("seg_start", ROWE)
    m.seg_inside = sb("seg_inside", ROWE)
    m.head_keep = sb("head_keep", ROWE)
    m.row_neg = sb("row_neg", P)
    m.row_inside = sb("row_inside", P)
    m.alpha = sb("alpha", NBLK * 8)
    m.w_self = sb("w_self", NBLK * 12)
    m.edge_w = sb("edge_w", NT * 12)
    m.weights = sb("weights", 3200)
    m.post = sb("post", 2340)
    m.shared = sb("shared", 15600)
    m.agg = nc.alloc_psum_tensor("agg", [P, 2, 512], F32)[:, :, :]
    m.pa = nc.alloc_psum_tensor("pa", [P, 512], F32)[:, :]
    m.pb = nc.alloc_psum_tensor("pb", [P, 512], F32)[:, :]
    m.kv = nc.alloc_psum_tensor("kv", [P, 512], F32)[:, :]
    m.vs = nc.alloc_psum_tensor("vs", [P, 512], F32)[:, :]

    m.gathered = [Signal(nc, f"gathered{i}") for i in range(RING)]
    m.rows_ready = Signal(nc, "rows_ready")
    m.rows_free = Signal(nc, "rows_free")
    m.onehot_ready = Signal(nc, "onehot_ready")
    m.onehot_free = Signal(nc, "onehot_free")
    m.agg_done = Signal(nc, "agg_done")
    m.agg_free = Signal(nc, "agg_free")
    m.vec_to_pe = Signal(nc, "vec_to_pe")
    m.pe_to_vec = Signal(nc, "pe_to_vec")
    m.vec_to_act = Signal(nc, "vec_to_act")
    m.act_to_vec = Signal(nc, "act_to_vec")
    m.stored = Signal(nc, "stored")
    m.loaded = Signal(nc, "loaded")
    m.idx_copied = Signal(nc, "idx_copied")
    m.vec_to_store = Signal(nc, "vec_to_store")
    m.vec_to_pool = Signal(nc, "vec_to_pool")
    m.pool_to_vec = Signal(nc, "pool_to_vec")
    m.pool_step = Signal(nc, "pool_step")
    m.lo_loaded = Signal(nc, "lo_loaded")
    m.lo_used = Signal(nc, "lo_used")
    m.lo_onehot = Signal(nc, "lo_onehot")
    m.gsum_ready = Signal(nc, "gsum_ready")
    m.gsum_free = Signal(nc, "gsum_free")
    m.self_loaded = Signal(nc, "self_loaded")
    m.self_ready = Signal(nc, "self_ready")
    m.self_used = Signal(nc, "self_used")
    m.qk_loaded = Signal(nc, "qk_loaded")
    m.qk_used = Signal(nc, "qk_used")
    m.moved = Signal(nc, "moved")
    m.sums_read = Signal(nc, "sums_read")

    m.lo_line = nc.dram_tensor("lo_line", [1, EPAD], BF16).ap()
    m.max_line = {H: nc.dram_tensor(f"max_line{H}_{k}", [EPAD, H], F32).ap() for k, H in enumerate((2, 4, 1))}
    m.inj_line = {H: nc.dram_tensor(f"inj_line{H}_{k}", [EPAD, 2 * H], F32).ap() for k, H in enumerate((2, 4, 1))}
    widths = [390, 780, 387, 384, 384, 384, 768, 768, 768]
    m.table = [nc.dram_tensor(f"table{i}", [NPAD, w], BF16).ap() for i, w in enumerate(widths)]
    m.q_line = nc.dram_tensor("q_line", [NBLK * P, 256], F32).ap()
    m.k_line = nc.dram_tensor("k_line", [NBLK * P, 257], F32).ap()
    return m


def flat(ap):
    return ap.rearrange("p a b -> p (a b)")


def split3(v, src, hi, mid, lo, rest):
    v.tensor_copy(hi, src)
    v.drain()
    v.tensor_tensor(rest, src, hi, ALU.subtract)
    v.drain()
    v.tensor_copy(mid, rest)
    v.drain()
    v.tensor_tensor(lo, rest, mid, ALU.subtract)
    v.drain()


def setup(nc, m, src, dst):
    c = Carve(m.shared)
    src_i = c.take([ROWE], I32)
    dst_i = c.take([ROWE], I32)
    prev_i = c.take([ROWE], I32)
    lo_i = c.take([ROWE], I32)
    hi_i = c.take([ROWE], I32)
    src_f = c.take([ROWE])
    dst_r = c.take([ROWE])
    prev_r = c.take([ROWE])
    hi_f = c.take([ROWE])
    lo_b = c.take([ROWE], BF16)
    any_col = c.take([8])
    dcol_i = c.take([NT], I32)
    dlo_i = c.take([NT], I32)
    dhi_i = c.take([NT], I32)
    c2 = Carve(m.edge_w)
    dlo_b = c2.take([NT], BF16)
    dhi_b = c2.take([NT], BF16)
    lo_hot = c2.take([2 * 8, P], BF16)
    hi_hot = c2.take([2 * 8, NBLK], BF16)
    tri = c2.take([P])
    tot = c2.take([NBLK])
    off = c2.take([64])
    ptr = c2.take([NBLK])
    zero_f = c2.take([1024])
    R = ROWS

    def rows(line, a, n, lead=0):
        return line[a * ROWE - lead:a * ROWE - lead + n * ROWE].rearrange("(r c) -> r c", c=ROWE)

    def cell(line, a, n):
        return line[a:a + n].rearrange("(r c) -> r c", r=1)

    with nc.Block() as block:
        @block.sync
        def _(sp):
            sp.wait_ge(m.vec_to_store.sem, 1)
            load = m.loaded.sem
            for to, line in ((src_i, src), (dst_i, dst)):
                sp.dma_start(to[0:FULL_ROWS, :], rows(line, 0, FULL_ROWS)).then_inc(load, 16)
                sp.dma_start(to[FULL_ROWS:R, 0:TAIL], cell(line, FULL_ROWS * ROWE, TAIL)).then_inc(load, 16)
            sp.dma_start(prev_i[0:1, 1:ROWE], cell(dst, 0, ROWE - 1)).then_inc(load, 16)
            sp.dma_start(prev_i[1:FULL_ROWS, :], rows(dst, 1, FULL_ROWS - 1, lead=1)).then_inc(load, 16)
            sp.dma_start(prev_i[FULL_ROWS:R, 0:TAIL + 1],
                         cell(dst, FULL_ROWS * ROWE - 1, TAIL + 1)).then_inc(load, 16)
            sp.wait_ge(m.vec_to_store.sem, 2)
            sp.dma_start(m.lo_line[0, :].rearrange("(r c) -> r c", c=ROWE), lo_b[0:R, :]).then_inc(m.stored.sem, 16)
            for H in (2, 4, 1):
                flat_line = m.inj_line[H].rearrange("(a b) c -> a (b c)", a=112)
                width = flat_line.shape[1]
                for at in range(0, width, 1024):
                    n = min(1024, width - at)
                    sp.dma_start(flat_line[:, at:at + n], zero_f[0:112, 0:n]).then_inc(m.stored.sem, 16)
            sp.wait_ge(m.stored.sem, 16 * (1 + sum(-(-ROWE * 2 * H // 1024) for H in (2, 4, 1))))

        @block.gpsimd
        def _(p):
            p.iota(m.iota_n, [[1, NPAD]], base=0, channel_multiplier=0)
            p.iota(m.iota_p[:, 0:1], [[0, 1]], base=0, channel_multiplier=1, allow_small_or_imprecise_dtypes=True)
            p.iota(m.iota_c, [[1, P]], base=0, channel_multiplier=0, allow_small_or_imprecise_dtypes=True)
            p.memset(m.ident, 0.0)
            p.memset(m.ident_b, 0.0)
            p.memset(m.mask, 1.0)
            p.memset(tri, 1.0)
            p.memset(m.ones, 1.0)
            p.memset(m.zero, 0.0).then_inc(m.pool_step.sem, 1)
            p.wait_ge(m.pool_step.sem, 1)
            for t in (m.ident, m.ident_b):
                p.affine_select(out=t, in_=t, compare_op=ALU.not_equal, fill=1.0, base=0,
                                pattern=[[-1, P]], channel_multiplier=1)
            p.affine_select(out=m.mask, in_=m.mask, compare_op=ALU.is_ge, fill=0.0, base=N - 1,
                            pattern=[[-P, NBLK]], channel_multiplier=-1)
            p.affine_select(out=tri, in_=tri, compare_op=ALU.is_gt, fill=0.0, base=0,
                            pattern=[[1, P]], channel_multiplier=-1)
            p.drain().then_inc(m.pool_to_vec.sem, 1)

        @block.vector
        def _(v):
            v.memset(zero_f, 0.0)
            v.memset(src_i, 0)
            v.memset(dst_i, 8000)
            v.memset(prev_i, 8000)
            v.drain()
            v.memset(prev_i[0:1, 0:1], -1)
            v.drain().then_inc(m.vec_to_store.sem, 1)
            v.wait_ge(m.loaded.sem, 7 * 16)
            v.tensor_scalar(hi_i[0:R, :], src_i[0:R, :], 7, None, ALU.logical_shift_right)
            v.tensor_scalar(lo_i[0:R, :], src_i[0:R, :], P - 1, None, ALU.bitwise_and)
            v.tensor_copy(src_f[0:R, :], src_i[0:R, :])
            v.tensor_copy(dst_r[0:R, :], dst_i[0:R, :])
            v.tensor_copy(prev_r[0:R, :], prev_i[0:R, :])
            v.drain()
            v.tensor_copy(hi_f[0:R, :], hi_i[0:R, :])
            v.tensor_copy(lo_b[0:R, :], lo_i[0:R, :])
            v.tensor_tensor(m.seg_start[0:R, :], dst_r[0:R, :], prev_r[0:R, :], ALU.not_equal)
            v.drain().then_inc(m.vec_to_store.sem, 1)
            v.tensor_scalar(m.seg_inside[0:R, :], m.seg_start[0:R, :], -1.0, 1.0, ALU.mult, ALU.add)
            v.tensor_tensor_scan(m.head_keep[0:R, :], m.seg_start[0:R, :], m.seg_start[0:R, :], 0.0, ALU.max, ALU.max)
            v.tensor_reduce(any_col[0:R, 0:1], m.seg_start[0:R, :], AX, ALU.max)
            v.drain()
            v.tensor_scalar(m.head_keep[0:R, :], m.head_keep[0:R, :], -1.0, 1.0, ALU.mult, ALU.add)
            for j in range(1, 8):
                v.tensor_copy(any_col[0:R, j:j + 1], any_col[0:R, 0:1])
            v.drain().then_inc(m.vec_to_pe.sem, 1)

            for n, (what, to) in enumerate(((src_f, m.src_idx), (hi_f, m.src_hi), (dst_r, m.dst_f))):
                for k in range(ROWT):
                    ps = (m.pa, m.pb)[(n * ROWT + k) % 2]
                    v.wait_ge(m.pe_to_vec.sem, n * ROWT + k + 1)
                    v.tensor_copy(to[:, k:NT:ROWT], ps[:, 0:R])
                    v.drain().then_inc(m.vec_to_pe.sem, 1)
            v.wait_ge(m.pe_to_vec.sem, 3 * ROWT + 1)
            v.tensor_scalar(m.row_neg[0:8, 0:R], m.pa[0:8, 0:R], NEG, None, ALU.mult)
            v.tensor_scalar(m.row_inside[0:8, 0:R], m.pa[0:8, 0:R], -1.0, 1.0, ALU.mult, ALU.add)
            v.tensor_copy(dcol_i, m.dst_f)
            v.drain()
            v.tensor_scalar(dhi_i, dcol_i, 7, None, ALU.logical_shift_right)
            v.tensor_scalar(dlo_i, dcol_i, P - 1, None, ALU.bitwise_and)
            v.drain()
            v.tensor_copy(dhi_b, dhi_i)
            v.tensor_copy(dlo_b, dlo_i)
            v.drain()
            v.wait_ge(m.pool_to_vec.sem, 1)
            with v.Fori(0, NT // 16) as j:
                for half in range(2):
                    v.wait_ge(m.onehot_free.sem, 2 * j + half + 1)
                    lo8 = lo_hot[:, half * 8:half * 8 + 8, :]
                    hi8 = hi_hot[:, half * 8:half * 8 + 8, :]
                    dlo = dlo_b[:, ds(j * 16 + half * 8, 8)].unsqueeze(2)
                    dhi = dhi_b[:, ds(j * 16 + half * 8, 8)].unsqueeze(2)
                    v.tensor_tensor(lo8, m.iota_c.unsqueeze(1).to_broadcast([P, 8, P]),
                                    dlo.to_broadcast([P, 8, P]), ALU.is_equal)
                    v.tensor_tensor(hi8, m.iota_c[:, 0:NBLK].unsqueeze(1).to_broadcast([P, 8, NBLK]),
                                    dhi.to_broadcast([P, 8, NBLK]), ALU.is_equal)
                    v.drain().then_inc(m.onehot_ready.sem, 1)
            v.wait_ge(m.agg_done.sem, 1)
            v.tensor_copy(m.deg, m.pa[:, 0:NBLK])
            v.drain().then_inc(m.vec_to_pe.sem, 1)
            v.wait_ge(m.agg_done.sem, 2)
            v.tensor_copy(tot, m.pb[:, 64:64 + NBLK])
            v.memset(off, 0.0)
            v.drain()
            v.tensor_tensor_scan(off[:, 1:NBLK + 1], m.ones[:, 0:NBLK], tot, 0.0, ALU.mult, ALU.add)
            v.drain()
            v.tensor_tensor(ptr, m.pb[:, 0:NBLK], off[:, 0:NBLK], ALU.add)
            v.tensor_copy(m.first_tile, off)
            v.tensor_scalar(m.has, m.deg, 0.0, None, ALU.is_gt)
            v.tensor_scalar(m.deg_inv, m.deg, 1.0, None, ALU.max)
            v.drain()
            v.tensor_scalar(m.first_tile, m.first_tile, 7, None, ALU.logical_shift_right)
            v.reciprocal(m.deg_inv, m.deg_inv)
            v.tensor_scalar(tot, m.has, -float(BIG_INDEX), float(BIG_INDEX), ALU.mult, ALU.add)
            v.tensor_tensor(off[:, 0:NBLK], ptr, m.deg, ALU.add)
            v.drain()
            v.tensor_tensor(tot, tot, ptr, ALU.add)
            v.tensor_scalar(off[:, 0:NBLK], off[:, 0:NBLK], -1.0, 0.0, ALU.add, ALU.max)
            v.drain()
            v.tensor_copy(m.start_idx, tot)
            v.tensor_copy(m.last_idx, off[:, 0:NBLK])
            v.drain()

        @block.tensor
        def _(pe):
            pe.wait_ge(m.pool_to_vec.sem, 1)
            for n, what in enumerate((src_f, hi_f, dst_r)):
                for k in range(ROWT):
                    ps = (m.pa, m.pb)[(n * ROWT + k) % 2]
                    pe.wait_ge(m.vec_to_pe.sem, max(1, n * ROWT + k))
                    pe.transpose(ps[:, 0:R], what[0:R, k * P:(k + 1) * P],
                                 m.ident[0:R, 0:R]).then_inc(m.pe_to_vec.sem, 1)
            pe.wait_ge(m.vec_to_pe.sem, 1 + 3 * ROWT)
            pe.transpose(m.pa[0:8, 0:R], any_col[0:R, 0:8], m.ident[0:R, 0:R]).then_inc(m.pe_to_vec.sem, 1)
            pe.sem_inc(m.onehot_free.sem, 2)
            pe.wait_ge(m.onehot_ready.sem, 1)
            pe.matmul(m.pa[:, 0:NBLK], m.zero[:, 0:P], m.zero[:, 0:NBLK], start=True, stop=True)
            with pe.Fori(0, NT // 16) as j:
                for half in range(2):
                    pe.wait_ge(m.onehot_ready.sem, 2 * j + half + 1)
                    for i in range(half * 8, half * 8 + 8):
                        last = pe.matmul(m.pa[:, 0:NBLK], lo_hot[:, i, :], hi_hot[:, i, :], start=False, stop=True,
                                         skip_group_check=True)
                    last.then_inc(m.onehot_free.sem, 1)
            pe.matmul(m.pa[:, 0:1], m.zero[:, 0:P], m.zero[:, 0:1], start=False, stop=True,
                      skip_group_check=True).then_inc(m.agg_done.sem, 1)
            pe.wait_ge(m.vec_to_pe.sem, 2 + 3 * ROWT)
            pe.matmul(m.pb[:, 0:NBLK], tri, m.deg, start=True, stop=True)
            pe.matmul(m.pb[:, 64:64 + NBLK], m.ones, m.deg, start=True, stop=True).then_inc(m.agg_done.sem, 1)

    m.vec_to_store.ended(2)
    m.loaded.ended(7 * 16)
    m.stored.ended(16 * (1 + sum(-(-ROWE * 2 * H // 1024) for H in (2, 4, 1))))
    m.pool_step.ended(1)
    m.pool_to_vec.ended(1)
    m.vec_to_pe.ended(2 + 3 * ROWT)
    m.pe_to_vec.ended(3 * ROWT + 1)
    m.onehot_ready.ended(NT // 8)
    m.onehot_free.ended(NT // 8 + 2)
    m.agg_done.ended(2)


class NodeSteps:

    def __init__(self, b, sig, per_block):
        self.b, self.sig, self.per, self.n = b, sig, per_block, 0

    def give(self, ins):
        ins.then_inc(self.sig.sem, 1)
        self.n += 1

    def wait(self, eng):
        self.n += 1
        eng.wait_ge(self.sig.sem, self.sig.past + self.b * self.per + self.n)


def vec_layer_norm(v, x, out, stat, to_act, from_act, extra=None):
    v.bn_stats(stat[:, 0:6], x)
    v.drain()
    v.bn_aggr(stat[:, 6:8], stat[:, 0:6])
    v.drain()
    v.tensor_scalar(stat[:, 8:9], stat[:, 7:8], EPS, None, ALU.add)
    to_act.give(v.drain())
    from_act.wait(v)
    v.reciprocal(stat[:, 10:11], stat[:, 9:10])
    v.drain()
    v.tensor_scalar(out, x, stat[:, 6:7], stat[:, 10:11], ALU.subtract, ALU.mult)
    v.drain()


def act_layer_norm(a, stat, to_vec, from_vec):
    from_vec.wait(a)
    to_vec.give(a.activation(stat[:, 9:10], stat[:, 8:9], ACT.Sqrt))


class Layout:

    def __init__(self, m, i):
        c = Carve(m.shared)
        self.acc = c.take([NBLK, D])
        self.rows_base = c.take([RING * 780], BF16)
        self.oh = c.take([OH_MATS * P], BF16)
        c = Carve(m.post)
        self.stat = c.take([16])
        self.nd = c.take({0: [2, 65], 1: [4, 65]}.get(i, [1, 129]))
        self.rd = c.take([4])
        self.o = c.take([256])
        self.hs = c.take([D])
        self.rest = c.take([264])
        self.t = c.take([2, 129])
        self.ht = c.take([2, P])
        self.tb = c.take([780], BF16)
        self.self_rows = c.take([780], BF16)
        self.wt = Carve(m.weights)
        c = Carve(m.edge_w)
        if i >= 4:
            self.ks = c.take([257])
            self.qn = c.take([256])
            self.qt = c.take([2, P])
            self.qk = c.take([512])
            self.sq = c.take([512])
            self.kvs = c.take([2, 129])
            self.vss = c.take([2, 129])
            self.wq = c.take([256])
            self.wk = c.take([256])
            self.bqk = c.take([512])
            self.wo = c.take([10, D])
            self.bo = c.take([D])


PARTS = [(0, 195), (0, 130), (0, 65)]


def edge_pass(nc, m, i, a, out):
    heads = (2, 4, 1, 0, 0, 0, 0, 0, 0)[i]
    width = m.table[i].shape[1]
    mats = max(1, 3 * heads)
    slots = {1: 16, 3: 16, 6: 8, 12: 4}[mats]
    with_self = i in (1, 2)
    L = Layout(m, i)
    rows = L.rows_base[:, 0:RING * width]
    oh = L.oh
    halves = [(0, 390), (1, 390)] if i == 1 else [(0, width)] if width <= 390 else [(0, 384), (1, 384)]
    layer3 = i >= 5
    c65 = 129 if i == 2 else 65

    n_va = (2, 0, 1, 0, 2, 0, 0, 0, 0)[i]
    n_vp = {0: 2, 1: 2, 2: 0, 3: 2, 4: 5, 5: 2, 6: 2, 7: 2, 8: 2}[i]
    n_pv = {0: 2, 1: 2, 2: 0, 3: 2, 4: 5, 5: 3, 6: 3, 7: 3, 8: 3}[i]
    stores_out = i == 8

    W = L.wt
    if i == 0:
        w_x = W.take([264]); bias = W.take([D]); gamma = W.take([D]); beta = W.take([D])
    elif i == 1:
        W.take([264]); w2x = W.take([2, 130]); bias = W.take([256])
    elif i == 2:
        bias = W.take([D])
    elif i in (3, 4):
        w_l = W.take([D]); w_r = W.take([D]); bias = W.take([D])
    if with_self:
        W.take([1024 - W.at]) if W.at < 1024 else None
        self_oh = W.take([12 * P], BF16)

    def mat(slot_it, j):
        return oh[:, ds((slot_it % slots) * (mats * P) + j * P, P)]

    def row(slot, a0, n):
        return rows[:, ds(slot * width + a0, n)]

    with nc.Block() as block:
        @block.sync
        def _(sp):
            sp.sem_inc(m.rows_ready.sem, RING)
            with sp.Fori(0, NT // RING) as j:
                for s in range(RING):
                    sp.wait_ge(m.gathered[s].sem, m.gathered[s].past + j * 16 + 16)
                    sp.sem_inc(m.rows_ready.sem, 1)

        @block.gpsimd
        def _(p):
            ix = m.idx_stage
            with p.Fori(0, NT // RING) as j:
                for s in range(RING):
                    t = j * RING + s
                    if s % HALF == 0:
                        p.wait_ge(m.rows_ready.sem, m.rows_ready.past + t - HALF + RING)
                        p.tensor_copy(ix[:, s:s + HALF], m.src_idx[:, ds(t, HALF)]).then_inc(m.idx_copied.sem, 1)
                        p.wait_ge(m.idx_copied.sem, m.idx_copied.past + j * 2 + s // HALF + 1)
                    p.wait_ge(m.rows_free.sem, m.rows_free.past + t + 1)
                    p.nop(nofuse=True)
                    p.indirect_dma_start(rows[:, s * width:(s + 1) * width], None, m.table[i],
                                         bass.IndirectOffsetOnAxis(ap=ix[:, s:s + 1], axis=0)
                                         ).then_inc(m.gathered[s].sem, 16)

        @block.vector
        def _(v):
            if layer3:
                v.tensor_copy(flat(L.kvs), m.kv[:, 0:258])
                v.memset(L.vss[0:1, :, :], float(N))
                v.drain()
                v.tensor_copy(L.vss[0:1, :, 0:128], m.vs[0:1, 0:256].rearrange("p (a b) -> p a b", b=128))
                v.drain().then_inc(m.sums_read.sem, 1)
            if i in (0, 1):
                nh, nc_ = ((4, 65), (1, 129))[i]
                tbv = L.tb[:, 0:nh * 3 * nc_].rearrange("p (h k c) -> p h k c", k=3, c=nc_)
                v.memset(tbv[:, :, :, nc_ - 1:nc_], 0.0)
                v.drain()
                v.memset(tbv[:, :, 0, nc_ - 1:nc_], 1.0)
            if i in (4, 5, 6, 7):
                v.memset(L.t[:, :, 128:129], 1.0)
            v.drain()
            with v.Fori(0, NBLK) as b:
                f0 = v.value_load(m.first_tile[0:1, ds(b, 1)], min_val=0, max_val=LAST_TILE)
                f1 = v.value_load(m.first_tile[0:1, ds(b + 1, 1)], min_val=0, max_val=LAST_TILE)
                node = m.iota_n[:, ds(b * P, P)]
                to_act = NodeSteps(b, m.vec_to_act, n_va)
                from_act = NodeSteps(b, m.act_to_vec, n_va)
                to_pe = NodeSteps(b, m.vec_to_pe, n_vp)
                from_pe = NodeSteps(b, m.pe_to_vec, n_pv)
                if with_self:
                    v.wait_ge(m.self_used.sem, m.self_used.past + b + 1)
                    for j in range(mats):
                        v.tensor_scalar(self_oh[:, j * P:(j + 1) * P], m.ident_b,
                                        m.w_self[:, ds(b * mats + j, 1)], None, ALU.mult)
                    v.drain().then_inc(m.self_ready.sem, 1)

                def hot(t):
                    v.wait_ge(m.onehot_free.sem, m.onehot_free.past + t + b + 1)
                    for j in range(mats):
                        last = v.tensor_scalar(mat(t + b, j), node, m.dst_f[:, ds(t, 1)],
                                               m.edge_w[:, ds(t * mats + j, 1)] if heads else None,
                                               ALU.is_equal, *([ALU.mult] if heads else []))
                    last.then_inc(m.onehot_ready.sem, 1)

                with v.If(f1 > f0):
                    with v.Fori(f0, f1) as t:
                        hot(t)
                v.nop()
                hot(f1)

                v.wait_ge(m.agg_done.sem, m.agg_done.past + b + 1)
                if heads:
                    hb = min(heads, 2)
                    for bank, n in halves:
                        v.tensor_reduce(L.nd[:, bank * 2:bank * 2 + hb, :],
                                        m.agg[:, bank, 0:n].rearrange("p (h k c) -> p h c k", k=3, c=c65), AX, ALU.add)
                else:
                    for bank, n in halves:
                        v.tensor_reduce(L.o[:, bank * D:bank * D + D],
                                        m.agg[:, bank, 0:n].rearrange("p (k c) -> p c k", k=3), AX, ALU.add)
                v.drain().then_inc(m.agg_free.sem, 1)
                if heads:
                    w = c65 - 1
                    v.tensor_scalar(L.rd[:, 0:heads], L.nd[:, :, w], 0.5, None, ALU.max)
                    v.drain()
                    v.reciprocal(L.rd[:, 0:heads], L.rd[:, 0:heads])
                    v.drain()
                    for h in range(heads):
                        v.tensor_scalar(L.o[:, h * w:(h + 1) * w], L.nd[:, h, 0:w], L.rd[:, h:h + 1], None, ALU.mult)
                    v.drain()
                    v.tensor_tensor(L.o[:, 0:heads * w], L.o[:, 0:heads * w], bias, ALU.add)
                    v.drain()
                xb = flat(m.x[:, ds(b, 1), :])
                hb_ = flat(m.h[:, ds(b, 1), :])
                accb = flat(L.acc[:, ds(b, 1), :])

                def next_norm():
                    vec_layer_norm(v, xb, L.hs, L.stat, to_act, from_act)
                    v.tensor_scalar(L.hs, L.hs, 0.0, None, ALU.max)
                    v.drain()

                def table_free():
                    v.wait_ge(m.stored.sem, m.stored.past + b * 16)

                def alphas(at, n):
                    v.tensor_copy(m.alpha[:, ds(b * 2 * n, 2 * n)], m.pb[:, at:at + 2 * n])

                if i == 0:
                    vec_layer_norm(v, L.o[:, 0:D], L.o[:, 0:D], L.stat, to_act, from_act)
                    v.tensor_tensor(L.o[:, 0:D], L.o[:, 0:D], gamma, ALU.mult)
                    v.drain()
                    v.tensor_tensor(L.o[:, 0:D], L.o[:, 0:D], beta, ALU.add)
                    v.drain()
                    v.tensor_tensor(xb, xb, L.o[:, 0:D], ALU.add)
                    v.drain()
                    next_norm()
                    v.tensor_copy(hb_, L.hs)
                    to_pe.give(v.drain())
                    from_pe.wait(v)
                    v.tensor_copy(L.ht[:, 0, :], m.pa[:, 0:P])
                    to_pe.give(v.drain())
                    table_free()
                    from_pe.wait(v)
                    alphas(256, 4)
                    tbv = L.tb.rearrange("p (h k c) -> p h k c", k=3, c=65)
                    split3(v, m.pb[:, 0:256].rearrange("p (h c) -> p h c", c=64), tbv[:, :, 0, 0:64], tbv[:, :, 1, 0:64],
                           tbv[:, :, 2, 0:64], L.rest[:, 0:256].rearrange("p (h c) -> p h c", c=64))
                    v.drain().then_inc(m.vec_to_store.sem, 1)
                elif i == 1:
                    v.scalar_tensor_tensor(L.o, L.o, SLOPE, L.o, ALU.mult, ALU.max)
                    to_pe.give(v.drain())
                    from_pe.wait(v)
                    v.tensor_copy(flat(L.ht), m.pa[:, 0:256])
                    to_pe.give(v.drain())
                    table_free()
                    from_pe.wait(v)
                    alphas(128, 1)
                    tbv = L.tb[:, 0:387].rearrange("p (k c) -> p k c", c=129)
                    split3(v, m.pb[:, 0:128], tbv[:, 0, 0:128], tbv[:, 1, 0:128], tbv[:, 2, 0:128], L.rest[:, 0:128])
                    v.drain().then_inc(m.vec_to_store.sem, 1)
                elif i == 2:
                    o = L.o[:, 0:D]
                    v.scalar_tensor_tensor(o, o, SLOPE, o, ALU.mult, ALU.max)
                    v.drain()
                    v.tensor_tensor(o, o, hb_, ALU.add)
                    v.drain()
                    v.tensor_tensor(xb, xb, o, ALU.add)
                    v.drain()
                    next_norm()
                    v.tensor_copy(hb_, L.hs)
                    table_free()
                    split3(v, L.hs, L.tb[:, 0:128], L.tb[:, 128:256], L.tb[:, 256:384], L.rest[:, 0:128])
                    v.drain().then_inc(m.vec_to_store.sem, 1)
                elif i in (3, 4):
                    own = hb_ if i == 3 else accb
                    v.tensor_scalar(L.o[:, 0:D], L.o[:, 0:D], m.deg_inv[:, ds(b, 1)], None, ALU.mult)
                    v.tensor_copy(L.hs, own)
                    to_pe.give(v.drain())
                    from_pe.wait(v)
                    v.tensor_copy(flat(L.ht), m.pa[:, 0:256])
                    to_pe.give(v.drain())
                    from_pe.wait(v)
                    v.tensor_tensor(L.o[:, 0:D], m.pb[:, 0:D], bias, ALU.add)
                    v.drain()
                    if i == 3:
                        v.tensor_scalar(L.hs, L.o[:, 0:D], 0.0, None, ALU.max)
                        v.drain()
                        v.tensor_copy(accb, L.hs)
                    else:
                        v.tensor_tensor(xb, xb, L.o[:, 0:D], ALU.add)
                        v.drain()
                        next_norm()
                        for h in range(2):
                            v.tensor_copy(L.t[:, h, 0:D], L.hs)
                        to_pe.give(v.drain())
                        from_pe.wait(v)
                        v.tensor_copy(L.ht[:, 0, :], m.pa[:, 0:P])
                        to_pe.give(v.drain())
                        from_pe.wait(v)
                        v.tensor_tensor(L.qk, m.pb, L.bqk, ALU.add)
                        v.tensor_copy(accb, m.pa[:, 256:384])
                        v.drain()
                        v.tensor_tensor(L.sq, L.qk, L.qk, ALU.mult)
                        v.drain()
                        v.tensor_reduce(L.rd, L.sq.rearrange("p (h c) -> p h c", c=D), AX, ALU.add)
                        to_act.give(v.drain())
                        from_act.wait(v)
                        v.reciprocal(L.rd, L.stat[:, 12:16])
                        v.drain()
                        v.tensor_scalar(L.rd[:, 2:4], L.rd[:, 2:4], m.mask[:, ds(b, 1)], None, ALU.mult)
                        v.drain()
                        v.wait_ge(m.qk_used.sem, m.qk_used.past + b * 32 + 1)
                        for h in range(2):
                            v.tensor_scalar(L.qn[:, h * D:(h + 1) * D], L.qk[:, h * D:(h + 1) * D], L.rd[:, h:h + 1],
                                            None, ALU.mult)
                            v.tensor_scalar(L.ks[:, h * D:(h + 1) * D], L.qk[:, 256 + h * D:256 + (h + 1) * D],
                                            L.rd[:, 2 + h:3 + h], None, ALU.mult)
                        v.tensor_copy(L.ks[:, 256:257], m.mask[:, ds(b, 1)])
                        to_pe.give(v.drain())
                        from_pe.wait(v)
                        v.tensor_copy(flat(L.qt), m.pa[:, 0:256])
                        v.drain()
                    table_free()
                    split3(v, L.hs, L.tb[:, 0:128], L.tb[:, 128:256], L.tb[:, 256:384], L.rest[:, 0:128])
                    v.drain().then_inc(m.vec_to_store.sem, 1)
                else:
                    nb = 1 if i == 5 else 2
                    v.tensor_scalar(L.o[:, 0:nb * D], L.o[:, 0:nb * D], m.deg_inv[:, ds(b, 1)], 0.5, ALU.mult, ALU.mult)
                    from_pe.wait(v)
                    nd = m.pb[:, 0:258].rearrange("p (h c) -> p h c", c=129)
                    v.reciprocal(L.rd[:, 0:2], nd[:, :, 128])
                    v.drain()
                    for h in range(2):
                        prop = L.o[:, (h % nb) * D:(h % nb) * D + D]
                        v.scalar_tensor_tensor(L.t[:, h, 0:D], nd[:, h, 0:D], L.rd[:, h:h + 1], prop, ALU.mult, ALU.add)
                    to_pe.give(v.drain())
                    from_pe.wait(v)
                    v.tensor_copy(flat(L.ht), m.pa[:, 0:256])
                    to_pe.give(v.drain())
                    if i < 8:
                        table_free()
                        tbv = L.tb[:, 0:768].rearrange("p (h k c) -> p h k c", k=3, c=D)
                        split3(v, L.t[:, :, 0:D], tbv[:, :, 0, :], tbv[:, :, 1, :], tbv[:, :, 2, :],
                               L.rest[:, 0:256].rearrange("p (h c) -> p h c", c=D))
                        v.drain().then_inc(m.vec_to_store.sem, 1)
                        from_pe.wait(v)
                        v.tensor_tensor(accb, accb, m.pb[:, 0:D], ALU.add)
                        v.drain()
                    else:
                        from_pe.wait(v)
                        v.tensor_tensor(L.hs, accb, m.pb[:, 0:D], ALU.add)
                        v.drain()
                        v.tensor_tensor(L.hs, L.hs, L.bo, ALU.add)
                        v.drain()
                        v.scalar_tensor_tensor(xb, L.hs, 0.5, xb, ALU.mult, ALU.add)
                        v.drain().then_inc(m.vec_to_store.sem, 1)

        @block.scalar
        def _(s):
            with s.Fori(0, NBLK) as b:
                to_vec = NodeSteps(b, m.act_to_vec, n_va)
                from_vec = NodeSteps(b, m.vec_to_act, n_va)
                if with_self:
                    s.wait_ge(m.self_used.sem, m.self_used.past + b + 1)
                    s.dma_start(L.self_rows[:, 0:width], m.table[i][ds(b * P, P), :]).then_inc(m.self_loaded.sem, 16)
                if layer3:
                    s.wait_ge(m.qk_used.sem, m.qk_used.past + b + 1)
                    s.dma_start(flat(L.qt), m.q_line[ds(b * P, P), :]).then_inc(m.qk_loaded.sem, 16)
                    s.dma_start(L.ks, m.k_line[ds(b * P, P), :]).then_inc(m.qk_loaded.sem, 16)
                for _n in range({0: 2, 2: 1, 4: 1}.get(i, 0)):
                    act_layer_norm(s, L.stat, to_vec, from_vec)
                if i == 4:
                    from_vec.wait(s)
                    to_vec.give(s.activation(L.stat[:, 12:16], L.rd, ACT.Sqrt))
                s.wait_ge(m.vec_to_store.sem, m.vec_to_store.past + b + 1)
                if i < 8:
                    s.dma_start(m.table[i + 1][ds(b * P, P), :],
                                L.tb[:, 0:m.table[i + 1].shape[1]]).then_inc(m.stored.sem, 16)
                else:
                    s.dma_start(out[ds(b * P, TAIL_NODES), :],
                                flat(m.x[0:TAIL_NODES, ds(b, 1), :])).then_inc(m.stored.sem, 16)
                if i == 4:
                    s.dma_start(m.q_line[ds(b * P, P), :], flat(L.qt)).then_inc(m.qk_used.sem, 16)
                    s.dma_start(m.k_line[ds(b * P, P), :], L.ks).then_inc(m.qk_used.sem, 16)
            if i == 4:
                s.wait_ge(m.qk_used.sem, m.qk_used.past + NBLK * 32 + 1)
            if i == 8:
                s.dma_start(out[0:(NBLK - 1) * P, :].rearrange("(b p) d -> p b d", p=P)[TAIL_NODES:P],
                            m.x[TAIL_NODES:P, 0:NBLK - 1, :]).then_inc(m.stored.sem, 16)
                s.wait_ge(m.stored.sem, m.stored.past + NBLK * 16 + 16)
            else:
                s.wait_ge(m.stored.sem, m.stored.past + NBLK * 16)

        @block.tensor
        def _(pe):
            if i == 0:
                pe.sem_inc(m.rows_free.sem, RING)
            pe.sem_inc(m.onehot_free.sem, slots)
            if with_self:
                pe.sem_inc(m.self_used.sem, 1)
            if i >= 4:
                pe.sem_inc(m.qk_used.sem, 1)
            if layer3:
                pe.wait_ge(m.sums_read.sem, m.sums_read.past + 1)
            if 4 <= i < 8:
                pe.matmul(m.kv[:, 0:258], m.zero[:, 0:P], m.zero[:, 0:258], start=True, stop=True)
                pe.matmul(m.vs[:, 0:256], m.zero[:, 0:P], m.zero[:, 0:256], start=True, stop=True)

            def accumulate(mats_of, row_of):
                if heads:
                    for h in range(heads):
                        for k in range(3):
                            n = (3 - k) * c65
                            at = (h % 2) * 3 * c65
                            last = pe.matmul(m.agg[:, h // 2, at:at + n], mats_of(3 * h + k), row_of(h * 3 * c65, n),
                                             start=False, stop=True, skip_group_check=True)
                else:
                    for bank, n in halves:
                        last = pe.matmul(m.agg[:, bank, 0:n], mats_of(0), row_of(bank * 384, n),
                                         start=False, stop=True, skip_group_check=True)
                return last

            def fence():
                return pe.matmul(m.agg[:, 0, 0:1], m.zero[:, 0:P], m.zero[:, 0:1], start=False, stop=True,
                                 skip_group_check=True)

            with pe.Fori(0, NBLK) as b:
                f0 = pe.value_load(m.first_tile[0:1, ds(b, 1)], min_val=0, max_val=LAST_TILE)
                f1 = pe.value_load(m.first_tile[0:1, ds(b + 1, 1)], min_val=0, max_val=LAST_TILE)
                to_vec = NodeSteps(b, m.pe_to_vec, n_pv)
                from_vec = NodeSteps(b, m.vec_to_pe, n_vp)
                pe.wait_ge(m.agg_free.sem, m.agg_free.past + b)
                for bank, n in halves:
                    pe.matmul(m.agg[:, bank, 0:n], m.zero[:, 0:P], m.zero[:, 0:n], start=True, stop=True)

                if with_self:
                    pe.wait_ge(m.self_ready.sem, m.self_ready.past + b + 1)
                    pe.wait_ge(m.self_loaded.sem, m.self_loaded.past + b * 16 + 16)
                    accumulate(lambda j: self_oh[:, j * P:(j + 1) * P], lambda at, n: L.self_rows[:, at:at + n])
                    fence().then_inc(m.self_used.sem, 1)

                def tile(t):
                    pe.wait_ge(m.rows_ready.sem, m.rows_ready.past + RING + t + 1)
                    pe.wait_ge(m.onehot_ready.sem, m.onehot_ready.past + t + b + 1)
                    accumulate(lambda j: mat(t + b, j), lambda at, n: row(t % RING, at, n)
                               ).then_inc(m.onehot_free.sem, 1)

                with pe.If(f1 > f0):
                    with pe.Fori(f0, f1) as t:
                        tile(t)
                        fence().then_inc(m.rows_free.sem, 1)
                pe.nop()
                tile(f1)
                fence().then_inc(m.agg_done.sem, 1)

                if i == 0:
                    from_vec.wait(pe)
                    to_vec.give(pe.transpose(m.pa[:, 0:P], L.hs, m.ident))
                    from_vec.wait(pe)
                    to_vec.give(pe.matmul(m.pb[:, 0:264], L.ht[:, 0, :], w_x, start=True, stop=True))
                elif i == 1:
                    from_vec.wait(pe)
                    pe.transpose(m.pa[:, 0:P], L.o[:, 0:P], m.ident)
                    to_vec.give(pe.transpose(m.pa[:, P:2 * P], L.o[:, P:2 * P], m.ident))
                    from_vec.wait(pe)
                    pe.matmul(m.pb[:, 0:130], L.ht[:, 0, :], w2x[:, 0, :], start=True, stop=False)
                    to_vec.give(pe.matmul(m.pb[:, 0:130], L.ht[:, 1, :], w2x[:, 1, :], start=False, stop=True))
                elif i in (3, 4):
                    from_vec.wait(pe)
                    pe.transpose(m.pa[:, 0:P], L.o[:, 0:P], m.ident)
                    to_vec.give(pe.transpose(m.pa[:, P:2 * P], L.hs, m.ident))
                    from_vec.wait(pe)
                    pe.matmul(m.pb[:, 0:D], L.ht[:, 0, :], w_l, start=True, stop=False)
                    to_vec.give(pe.matmul(m.pb[:, 0:D], L.ht[:, 1, :], w_r, start=False, stop=True))
                    if i == 4:
                        from_vec.wait(pe)
                        to_vec.give(pe.transpose(m.pa[:, 0:P], L.hs, m.ident))
                        from_vec.wait(pe)
                        pe.matmul(m.pb[:, 0:256], L.ht[:, 0, :], L.wq, start=True, stop=True)
                        pe.matmul(m.pb[:, 256:512], L.ht[:, 0, :], L.wk, start=True, stop=True)
                        pe.matmul(m.pa[:, 256:384], L.ht[:, 0, :], L.wo[:, 0, :], start=True, stop=False)
                        to_vec.give(pe.matmul(m.pa[:, 256:384], L.ht[:, 0, :], L.wo[:, 5, :], start=False, stop=True))
                        from_vec.wait(pe)
                        for h in range(2):
                            pe.matmul(m.kv[:, h * 129:(h + 1) * 129], L.ks[:, h * D:(h + 1) * D], L.t[:, h, :],
                                      start=False, stop=True, skip_group_check=True)
                            pe.matmul(m.vs[0:1, h * D:(h + 1) * D], L.ks[:, 256:257], L.t[:, h, 0:D],
                                      start=False, stop=True, skip_group_check=True)
                        pe.transpose(m.pa[:, 0:P], L.qn[:, 0:P], m.ident)
                        to_vec.give(pe.transpose(m.pa[:, P:2 * P], L.qn[:, P:2 * P], m.ident))
                elif layer3:
                    pe.wait_ge(m.qk_loaded.sem, m.qk_loaded.past + b * 32 + 32)
                    for h in range(2):
                        pe.matmul(m.pb[:, h * 129:(h + 1) * 129], L.qt[:, h, :], L.kvs[:, h, :], start=True, stop=False)
                        last = pe.matmul(m.pb[:, h * 129:(h + 1) * 129], m.ones[0:1, 0:P], L.vss[0:1, h, :],
                                         start=False, stop=True)
                    to_vec.give(last)
                    from_vec.wait(pe)
                    pe.transpose(m.pa[:, 0:P], L.t[:, 0, 0:D], m.ident)
                    to_vec.give(pe.transpose(m.pa[:, P:2 * P], L.t[:, 1, 0:D], m.ident))
                    if i < 8:
                        for h in range(2):
                            pe.matmul(m.kv[:, h * 129:(h + 1) * 129], L.ks[:, h * D:(h + 1) * D], L.t[:, h, :],
                                      start=False, stop=True, skip_group_check=True)
                            pe.matmul(m.vs[0:1, h * D:(h + 1) * D], L.ks[:, 256:257], L.t[:, h, 0:D],
                                      start=False, stop=True, skip_group_check=True)
                    from_vec.wait(pe)
                    pe.matmul(m.pb[:, 0:D], L.ht[:, 0, :], L.wo[:, i - 4, :], start=True, stop=False)
                    to_vec.give(pe.matmul(m.pb[:, 0:D], L.ht[:, 1, :], L.wo[:, i + 1, :], start=False, stop=True))
                    pe.matmul(m.kv[:, 400:401], m.zero[:, 0:P], m.zero[:, 0:1], start=False, stop=True,
                              skip_group_check=True).then_inc(m.qk_used.sem, 1)
            pe.drain().then_inc(m.rows_free.sem, NT - LAST_TILE)

    for s in m.gathered:
        s.ended(NT // RING * 16)
    m.rows_ready.ended(NT + RING)
    m.rows_free.ended(NT)
    m.idx_copied.ended(NT // HALF)
    m.onehot_ready.ended(NBLK + LAST_TILE)
    m.onehot_free.ended(NBLK + LAST_TILE + slots)
    m.agg_done.ended(NBLK)
    m.agg_free.ended(NBLK)
    m.vec_to_pe.ended(NBLK * n_vp)
    m.pe_to_vec.ended(NBLK * n_pv)
    m.vec_to_act.ended(NBLK * n_va)
    m.act_to_vec.ended(NBLK * n_va)
    m.vec_to_store.ended(NBLK)
    m.stored.ended(16 * NBLK)
    if with_self:
        m.self_used.ended(NBLK + 1)
        m.self_ready.ended(NBLK)
        m.self_loaded.ended(16 * NBLK)
    if layer3:
        m.qk_used.ended(NBLK + 1)
        m.qk_loaded.ended(32 * NBLK)
        m.sums_read.ended(1)
    if i == 4:
        m.qk_used.ended(32 * NBLK + 1)


def edge_weights(nc, m, i):
    H = (2, 4, 1)[i]
    with_self = i > 0
    c = Carve(m.shared)
    el = c.take([NT, H])
    el_r = c.take([H, ROWE])
    tail_at = c.at
    lo_bc = c.take([2, CHUNK * P], BF16)
    lo_hot = c.take([2, CHUNK * P], BF16)
    prod = c.take([2, GCOLS])
    hi_hot = c.take([8, NBLK], BF16)
    tab = c.take([3 * H, NBLK], BF16)
    tab_rest = c.take([H, NBLK])
    c.at = tail_at
    inj = c.take([ROWE, 2 * H])
    max_r = inj.rearrange("p a b -> p (a b)")[:, 0:ROWE * H].rearrange("p (a b) -> p a b", b=H)
    seg_neg = c.take([ROWE])
    head_neg = Carve(m.weights).take([ROWE])
    c = Carve(m.post)
    last = c.take([8])
    chain = c.take([2 * P])
    carry = c.take([8])
    node_max = c.take([NBLK, H])
    node_m = c.take([NBLK, 2 * H])
    node_t = c.take([NBLK, H])
    neg_deg = c.take([NBLK])
    stage_idx = c.take([8], U32)
    stage_val = c.take([7, 2 * H])
    w_b = c.take([NBLK * H], BF16)
    c = Carve(m.weights)
    part = c.take([NT * H], BF16)
    alpha = m.alpha[:, 0:NBLK * 2 * H].rearrange("p (b j) -> p b j", j=2 * H)
    w_self = m.w_self[:, 0:NBLK * 3 * H].rearrange("p (b h k) -> p b h k", h=H, k=3)
    edge_w = m.edge_w[:, 0:NT * 3 * H].rearrange("p (t h k) -> p t h k", h=H, k=3)
    unit = 8 // H
    units = CHUNK // unit
    R = ROWS
    max_line, inj_line = m.max_line[H], m.inj_line[H]
    G = NBLK // 7

    with nc.Block() as block:
        @block.sync
        def _(sp):
            with sp.Fori(0, NCHUNK) as q:
                sp.wait_ge(m.lo_used.sem, m.lo_used.past + q + 1)
                sp.dma_start(lo_bc[:, ds(q % 2, 1), :].rearrange("p a b -> p (a b)"),
                             m.lo_line[0:1, ds(q * (CHUNK * P), CHUNK * P)].partition_broadcast(P)
                             ).then_inc(m.lo_loaded.sem, 16)
                sp.wait_ge(m.lo_loaded.sem, m.lo_loaded.past + q * 16 + 16)
                sp.nop(nofuse=True)
            sp.wait_ge(m.vec_to_store.sem, m.vec_to_store.past + 1)
            sp.dma_start(max_line.rearrange("(r c) h -> r (c h)", c=ROWE),
                         max_r[0:R].rearrange("p a b -> p (a b)")).then_inc(m.stored.sem, 16)
            sp.wait_ge(m.stored.sem, m.stored.past + 16)
            sp.sem_inc(m.pool_step.sem, 1)
            sp.wait_ge(m.pool_to_vec.sem, m.pool_to_vec.past + 2)
            sp.dma_start(inj[0:R].rearrange("p a b -> p (a b)"),
                         inj_line.rearrange("(r c) h -> r (c h)", c=ROWE)).then_inc(m.loaded.sem, 16)
            sp.wait_ge(m.loaded.sem, m.loaded.past + 16)

        @block.gpsimd
        def _(p):
            p.wait_ge(m.pool_step.sem, m.pool_step.past + 1)
            with p.Fori(0, G) as g:
                p.tensor_copy(stage_idx[:, 0:7], m.last_idx[:, ds(g * 7, 7)]).then_inc(m.idx_copied.sem, 1)
                p.wait_ge(m.idx_copied.sem, m.idx_copied.past + 2 * g + 1)
                p.nop(nofuse=True)
                for j in range(7):
                    p.indirect_dma_start(stage_val[:, j, 0:H], None, max_line,
                                         bass.IndirectOffsetOnAxis(ap=stage_idx[:, j:j + 1], axis=0)
                                         ).then_inc(m.moved.sem, 16)
                p.wait_ge(m.moved.sem, m.moved.past + g * 112 + 112)
                p.tensor_copy(node_max[:, ds(g * 7, 7), :], stage_val[:, :, 0:H]).then_inc(m.idx_copied.sem, 1)
                p.wait_ge(m.idx_copied.sem, m.idx_copied.past + 2 * g + 2)
                p.nop(nofuse=True)
            p.drain().then_inc(m.pool_to_vec.sem, 1)
            p.wait_ge(m.vec_to_pool.sem, m.vec_to_pool.past + 1)
            moved = m.moved.past + G * 112
            copied = m.idx_copied.past + 2 * G
            with p.Fori(0, G) as g:
                p.tensor_copy(stage_idx[:, 0:7], m.start_idx[:, ds(g * 7, 7)]).then_inc(m.idx_copied.sem, 1)
                p.tensor_copy(stage_val, node_m[:, ds(g * 7, 7), :]).then_inc(m.idx_copied.sem, 1)
                p.wait_ge(m.idx_copied.sem, copied + 2 * g + 2)
                p.nop(nofuse=True)
                for j in range(7):
                    p.indirect_dma_start(inj_line, bass.IndirectOffsetOnAxis(ap=stage_idx[:, j:j + 1], axis=0),
                                         stage_val[:, j, :], None, bounds_check=EPAD - 1, oob_is_err=False
                                         ).then_inc(m.moved.sem, 16)
                p.wait_ge(m.moved.sem, moved + g * 112 + 112)
                p.nop(nofuse=True)
            p.drain().then_inc(m.pool_to_vec.sem, 1)

        @block.vector
        def _(v):
            al = alpha[:, :, 0:H].rearrange("p b h -> p h b")
            split3(v, al, tab[:, 0:H, :], tab[:, H:2 * H, :], tab[:, 2 * H:3 * H, :], tab_rest)
            v.drain().then_inc(m.vec_to_pe.sem, 1)
            with v.Fori(0, NCHUNK) as q:
                v.wait_ge(m.lo_loaded.sem, m.lo_loaded.past + q * 16 + 16)
                v.tensor_scalar(lo_hot[:, ds(q % 2, 1), :].rearrange("p a b -> p (a b)"),
                                lo_bc[:, ds(q % 2, 1), :].rearrange("p a b -> p (a b)"),
                                m.iota_p[:, 0:1], None, ALU.is_equal).then_inc(m.lo_onehot.sem, 1)
                v.drain().then_inc(m.lo_used.sem, 1)
                for u in range(units):
                    t0 = q * CHUNK + u * unit
                    v.tensor_tensor(hi_hot[:, 0:unit, :],
                                    m.iota_c[:, 0:NBLK].unsqueeze(1).to_broadcast([P, unit, NBLK]),
                                    m.src_hi[:, ds(t0, unit)].unsqueeze(2).to_broadcast([P, unit, NBLK]),
                                    ALU.is_equal)
                    v.drain()
                    v.wait_ge(m.gsum_ready.sem, m.gsum_ready.past + q * units + u + 1)
                    ps = (m.pa, m.pb)[u % 2][:, 0:GCOLS].rearrange("p (t h b) -> p t h b", h=H, b=NBLK)
                    pr = prod[:, u % 2, :].rearrange("p (t h b) -> p t h b", h=H, b=NBLK)
                    v.tensor_tensor(pr, ps, hi_hot[:, 0:unit, :].unsqueeze(2).to_broadcast([P, unit, H, NBLK]),
                                    ALU.mult)
                    v.drain().then_inc(m.gsum_free.sem, 1)
                    v.tensor_reduce(el[:, ds(t0, unit), :], pr, AX, ALU.add)
            v.tensor_scalar(seg_neg[0:R, :], m.seg_start[0:R, :], NEG, None, ALU.mult)
            v.tensor_scalar(head_neg[0:R, :], m.head_keep[0:R, :], -NEG, NEG, ALU.mult, ALU.add)
            v.drain().then_inc(m.vec_to_pe.sem, 1)

            n = 0
            for h in range(H):
                for k in range(ROWT):
                    v.wait_ge(m.pe_to_vec.sem, m.pe_to_vec.past + n + 1)
                    v.tensor_copy(el_r[0:R, h, k * P:(k + 1) * P], (m.pa, m.pb)[n % 2][0:R, 0:P])
                    v.drain().then_inc(m.vec_to_pe.sem, 1)
                    n += 1
            to_pe = [2 + n]
            from_pe = [n]

            def give_pe():
                v.drain().then_inc(m.vec_to_pe.sem, 1)
                to_pe[0] += 1

            def wait_pe():
                from_pe[0] += 1
                v.wait_ge(m.pe_to_vec.sem, m.pe_to_vec.past + from_pe[0])

            def scan(cols, keep, value, result, row_keep, initial, op0, op1, head, head_op0):
                for j in range(cols):
                    v.tensor_tensor_scan(result(j), keep, value(j), initial, op0, op1)
                v.drain()
                for j in range(cols):
                    v.tensor_copy(last[0:R, j:j + 1], result(j)[:, ROWE - 1:ROWE])
                give_pe()
                wait_pe()
                v.memset(chain[0:cols, 0:1], initial)
                v.tensor_copy(chain[0:cols, P:P + R], m.pa[0:cols, 0:R])
                v.drain()
                v.tensor_tensor_scan(chain[0:cols, 1:R], row_keep[0:cols, 0:R - 1], chain[0:cols, P:P + R - 1],
                                     initial, op0, op1)
                give_pe()
                wait_pe()
                v.tensor_copy(carry[0:R, 0:cols], m.pb[0:R, 0:cols])
                v.drain()
                for j in range(cols):
                    v.scalar_tensor_tensor(result(j), head[0:R, :], carry[0:R, j:j + 1], result(j), head_op0, op1)
                v.drain()

            scan(H, seg_neg[0:R, :], lambda j: el_r[0:R, j, :], lambda j: max_r[0:R, :, j], m.row_neg, NEG,
                 ALU.add, ALU.max, head_neg, ALU.add)
            v.drain().then_inc(m.vec_to_store.sem, 1)

            v.tensor_scalar(neg_deg, m.has, -NEG, NEG, ALU.mult, ALU.add)
            v.wait_ge(m.pool_to_vec.sem, m.pool_to_vec.past + 1)
            hasb = m.has.unsqueeze(2).to_broadcast([P, NBLK, H])
            negb = neg_deg.unsqueeze(2).to_broadcast([P, NBLK, H])
            v.tensor_tensor(node_max, node_max, hasb, ALU.mult)
            v.tensor_copy(node_m[:, :, 0:H], alpha[:, :, H:2 * H])
            v.drain()
            v.tensor_tensor(node_max, node_max, negb, ALU.add)
            v.drain()
            v.tensor_tensor(node_max, node_max, alpha[:, :, H:2 * H], ALU.add)
            v.drain()
            v.scalar_tensor_tensor(node_max, node_max, SLOPE, node_max, ALU.mult, ALU.max)
            if with_self:
                v.tensor_tensor(node_t, alpha[:, :, 0:H], alpha[:, :, H:2 * H], ALU.add)
                v.drain()
                v.scalar_tensor_tensor(node_t, node_t, SLOPE, node_t, ALU.mult, ALU.max)
                v.drain()
                v.tensor_tensor(node_max, node_max, node_t, ALU.max)
                v.drain()
                v.tensor_tensor(node_t, node_t, node_max, ALU.subtract)
            v.drain()
            v.tensor_copy(node_m[:, :, H:2 * H], node_max)
            v.drain().then_inc(m.vec_to_pool.sem, 1)
            if with_self:
                v.drain().then_inc(m.vec_to_act.sem, 1)
                v.wait_ge(m.act_to_vec.sem, m.act_to_vec.past + 1)
                wb = w_b.rearrange("p (b h) -> p b h", h=H)
                for k in range(3):
                    v.tensor_copy(wb, node_t)
                    v.drain()
                    v.tensor_copy(w_self[:, :, :, k], wb)
                    if k < 2:
                        v.tensor_tensor(node_t, node_t, wb, ALU.subtract)
                    v.drain()

            v.wait_ge(m.loaded.sem, m.loaded.past + 16)
            for j in range(2 * H):
                v.tensor_tensor(inj[0:R, :, j], inj[0:R, :, j], m.seg_start[0:R, :], ALU.mult)
            v.drain()
            scan(2 * H, m.seg_inside[0:R, :], lambda j: inj[0:R, :, j], lambda j: inj[0:R, :, j], m.row_inside, 0.0,
                 ALU.mult, ALU.add, m.head_keep, ALU.mult)
            for h in range(H):
                v.tensor_tensor(el_r[0:R, h, :], el_r[0:R, h, :], inj[0:R, :, h], ALU.add)
            v.drain()
            v.scalar_tensor_tensor(el_r[0:R], el_r[0:R], SLOPE, el_r[0:R], ALU.mult, ALU.max)
            v.drain()
            for h in range(H):
                v.tensor_tensor(el_r[0:R, h, :], el_r[0:R, h, :], inj[0:R, :, H + h], ALU.subtract)
            v.drain()
            v.tensor_scalar(el_r[0:R], el_r[0:R], 0.0, None, ALU.min)
            v.drain().then_inc(m.vec_to_act.sem, 1)
            v.wait_ge(m.act_to_vec.sem, m.act_to_vec.past + (2 if with_self else 1))
            give_pe()
            for h in range(H):
                for k in range(ROWT):
                    wait_pe()
                    v.tensor_copy(el[:, k:NT:ROWT, h], (m.pa, m.pb)[(from_pe[0] + 1) % 2][:, 0:R])
                    give_pe()
            elf = el.rearrange("p a b -> p (a b)")
            for k in range(3):
                v.tensor_copy(part, elf)
                v.drain()
                v.tensor_copy(edge_w[:, :, :, k], part.rearrange("p (a b) -> p a b", b=H))
                if k < 2:
                    v.tensor_tensor(elf, elf, part, ALU.subtract)
                v.drain()
            v.drain()

        @block.scalar
        def _(s):
            n = 0
            if with_self:
                s.wait_ge(m.vec_to_act.sem, m.vec_to_act.past + 1)
                s.activation(node_t, node_t, ACT.Exp).then_inc(m.act_to_vec.sem, 1)
                n = 1
            s.wait_ge(m.vec_to_act.sem, m.vec_to_act.past + n + 1)
            s.activation(el_r[0:R], el_r[0:R], ACT.Exp).then_inc(m.act_to_vec.sem, 1)

        @block.tensor
        def _(pe):
            if i == 0:
                pe.sem_inc(m.lo_used.sem, 2)
                pe.sem_inc(m.gsum_free.sem, 2)
            pe.wait_ge(m.vec_to_pe.sem, m.vec_to_pe.past + 1)
            with pe.Fori(0, NCHUNK) as q:
                pe.wait_ge(m.lo_onehot.sem, m.lo_onehot.past + q + 1)
                for u in range(units):
                    ps = (m.pa, m.pb)[u % 2]
                    pe.wait_ge(m.gsum_free.sem, m.gsum_free.past + q * units + u + 1)
                    for j in range(unit):
                        lhs = lo_hot[:, ds(q % 2, 1), (u * unit + j) * P:(u * unit + j + 1) * P].rearrange("p a b -> p (a b)")
                        for k in range(3):
                            lastmm = pe.matmul(ps[:, j * H * NBLK:(j + 1) * H * NBLK], lhs,
                                               tab[:, k * H:(k + 1) * H, :].rearrange("p a b -> p (a b)"),
                                               start=(k == 0), stop=(k == 2))
                    lastmm.then_inc(m.gsum_ready.sem, 1)
            n = 0
            for h in range(H):
                for k in range(ROWT):
                    pe.wait_ge(m.vec_to_pe.sem, m.vec_to_pe.past + 2 + max(0, n - 1))
                    pe.transpose((m.pa, m.pb)[n % 2][0:R, 0:P], el[:, k:NT:ROWT, h], m.ident).then_inc(m.pe_to_vec.sem, 1)
                    n += 1
            got = 2 + n

            def carries(cols, got):
                pe.wait_ge(m.vec_to_pe.sem, m.vec_to_pe.past + got + 1)
                pe.transpose(m.pa[0:cols, 0:R], last[0:R, 0:cols], m.ident[0:R, 0:R]).then_inc(m.pe_to_vec.sem, 1)
                pe.wait_ge(m.vec_to_pe.sem, m.vec_to_pe.past + got + 2)
                pe.transpose(m.pb[0:R, 0:cols], chain[0:cols, 0:R], m.ident[0:cols, 0:cols]).then_inc(m.pe_to_vec.sem, 1)
                return got + 2

            got = carries(H, got)
            got = carries(2 * H, got)
            base = got + 1
            n2 = n + 4
            for h in range(H):
                for k in range(ROWT):
                    idx = h * ROWT + k
                    pe.wait_ge(m.vec_to_pe.sem, m.vec_to_pe.past + base + max(0, idx - 1))
                    pe.transpose((m.pa, m.pb)[(n2 + idx) % 2][:, 0:R], el_r[0:R, h, k * P:(k + 1) * P],
                                 m.ident[0:R, 0:R]).then_inc(m.pe_to_vec.sem, 1)

    n = H * ROWT
    m.lo_used.ended(NCHUNK)
    m.lo_loaded.ended(16 * NCHUNK)
    m.lo_onehot.ended(NCHUNK)
    m.gsum_ready.ended(NCHUNK * units)
    m.gsum_free.ended(NCHUNK * units)
    m.vec_to_store.ended(1)
    m.stored.ended(16)
    m.pool_step.ended(1)
    m.pool_to_vec.ended(2)
    m.loaded.ended(16)
    m.idx_copied.ended(4 * G)
    m.moved.ended(2 * G * 112)
    m.vec_to_pool.ended(1)
    m.vec_to_pe.ended(2 + n + 4 + 1 + n)
    m.pe_to_vec.ended(n + 4 + n)
    m.vec_to_act.ended(2 if with_self else 1)
    m.act_to_vec.ended(2 if with_self else 1)


def line(ap):
    return ap.rearrange("(o d) -> o d", o=1)


def table_init(nc, m, a):
    c = Carve(m.shared)
    tab = c.take([NBLK, 390], BF16)
    stats = c.take([6])
    mv_b = c.take([2])
    mv = c.take([NBLK, 2])
    sd = c.take([NBLK])
    rstd = c.take([NBLK])
    w_x = c.take([132])
    att = c.take([2, D])
    prod = c.take([2, D])
    stage = c.take([D])
    ht = c.take([P])
    rest = c.take([2, 64])
    whole = N // P
    with nc.Block() as block:
        @block.sync
        def _(sp):
            load = m.loaded.sem
            sp.wait_ge(m.vec_to_store.sem, m.vec_to_store.past + 1)
            for p0 in (0, P // 2):
                sp.dma_start(m.x[p0:p0 + P // 2, 0:whole, :],
                             a["x"][0:whole * P, :].rearrange("(b p) d -> p b d", p=P)[p0:p0 + P // 2]).then_inc(load, 16)
            sp.dma_start(m.x[0:N - whole * P, whole, :], a["x"][whole * P:N, :]).then_inc(load, 16)
            sp.dma_start(w_x[:, 0:D], a["L0_gnn_W"]).then_inc(load, 16)
            for j, name in enumerate(("L0_gnn_attn_l", "L0_gnn_attn_r")):
                sp.dma_start(att[:, j, :], line(a[name].rearrange("h d -> (h d)")).partition_broadcast(P)).then_inc(load, 16)
            sp.wait_ge(m.vec_to_store.sem, m.vec_to_store.past + 2)
            sp.dma_start(m.table[0].rearrange("(b p) w -> p b w", p=P), tab).then_inc(m.stored.sem, 16)
            sp.wait_ge(m.stored.sem, m.stored.past + 16)

        @block.vector
        def _(v):
            v.memset(m.x[:, whole, :], 0.0)
            v.drain().then_inc(m.vec_to_store.sem, 1)
            tv = tab.rearrange("p b (g c) -> p b g c", c=65)
            v.memset(tv[:, :, :, 64:65], 0.0)
            v.drain()
            v.memset(tv[:, :, 0:6:3, 64:65], 1.0)
            v.wait_ge(m.loaded.sem, m.loaded.past + 96)
            v.tensor_tensor(prod, att, w_x[:, 0:D].unsqueeze(1).to_broadcast([P, 2, D]), ALU.mult)
            v.drain()
            v.tensor_reduce(w_x[:, D:D + 4], prod.rearrange("p j (h c) -> p (j h) c", c=64), AX, ALU.add)
            with v.Fori(0, NBLK) as b:
                v.bn_stats(stats, flat(m.x[:, ds(b, 1), :]))
                v.drain()
                v.bn_aggr(mv_b, stats)
                v.drain()
                v.tensor_copy(flat(mv[:, ds(b, 1), :]), mv_b)
            v.drain()
            v.tensor_scalar(sd, mv[:, :, 1], EPS, None, ALU.add)
            v.drain().then_inc(m.vec_to_act.sem, 1)
            v.wait_ge(m.act_to_vec.sem, m.act_to_vec.past + 1)
            v.reciprocal(rstd, sd)
            v.drain()
            with v.Fori(0, NBLK) as b:
                v.tensor_scalar(flat(m.h[:, ds(b, 1), :]), flat(m.x[:, ds(b, 1), :]), flat(mv[:, ds(b, 1), 0:1]),
                                rstd[:, ds(b, 1)], ALU.subtract, ALU.mult)
            v.drain()
            v.tensor_scalar(flat(m.h), flat(m.h), 0.0, None, ALU.max)
            v.drain().then_inc(m.vec_to_act.sem, 1)
            with v.Fori(0, NBLK) as b:
                v.wait_ge(m.pe_to_vec.sem, m.pe_to_vec.past + b + 1)
                ps = flat(m.agg[:, ds(b % 2, 1), :])
                t1 = flat(tab[:, ds(b, 1), :]).rearrange("p (h k c) -> p h k c", k=3, c=65)
                v.tensor_copy(m.alpha[:, ds(b * 4, 4)], ps[:, D:D + 4])
                split3(v, ps[:, 0:D].rearrange("p (h c) -> p h c", c=64), t1[:, :, 0, 0:64], t1[:, :, 1, 0:64],
                       t1[:, :, 2, 0:64], rest)
                v.drain().then_inc(m.agg_free.sem, 1)
            v.drain().then_inc(m.vec_to_store.sem, 1)

        @block.scalar
        def _(s):
            s.wait_ge(m.vec_to_act.sem, m.vec_to_act.past + 1)
            s.activation(sd, sd, ACT.Sqrt).then_inc(m.act_to_vec.sem, 1)
            s.wait_ge(m.vec_to_act.sem, m.vec_to_act.past + 2)
            with s.Fori(0, NBLK) as b:
                s.activation(stage, flat(m.h[:, ds(b, 1), :]), ACT.Copy).then_inc(m.self_ready.sem, 1)
                s.wait_ge(m.gsum_ready.sem, m.gsum_ready.past + b + 1)
                s.wait_ge(m.pe_to_vec.sem, m.pe_to_vec.past + b)
                s.activation(ht, m.pa[:, 0:P], ACT.Copy).then_inc(m.lo_onehot.sem, 1)

        @block.tensor
        def _(pe):
            pe.sem_inc(m.agg_free.sem, 2)
            with pe.Fori(0, NBLK) as b:
                pe.wait_ge(m.self_ready.sem, m.self_ready.past + b + 1)
                pe.transpose(m.pa[:, 0:P], stage, m.ident).then_inc(m.gsum_ready.sem, 1)
                pe.wait_ge(m.lo_onehot.sem, m.lo_onehot.past + b + 1)
                pe.wait_ge(m.agg_free.sem, m.agg_free.past + b + 1)
                pe.matmul(m.agg[:, ds(b % 2, 1), 0:132].rearrange("p a b -> p (a b)"), ht, w_x,
                          start=True, stop=True).then_inc(m.pe_to_vec.sem, 1)

    m.vec_to_store.ended(2)
    m.loaded.ended(96)
    m.stored.ended(16)
    m.vec_to_act.ended(2)
    m.act_to_vec.ended(1)
    m.pe_to_vec.ended(NBLK)
    m.agg_free.ended(NBLK + 2)
    m.self_ready.ended(NBLK)
    m.gsum_ready.ended(NBLK)
    m.lo_onehot.ended(NBLK)


def prepare(nc, m, i, a):
    L = Layout(m, i)
    W = L.wt
    tmp = Carve(m.shared)
    tmp.at = NBLK * D
    loads = []

    def bcast(to, name):
        loads.append((to, line(a[name]).partition_broadcast(P)))

    att = prod = raw = None
    if i == 0:
        w_x = W.take([264])
        for name in ("L0_gnn_bias", "L0_gnn_gamma", "L0_gnn_beta"):
            bcast(W.take([D]), name)
        att, prod = tmp.take([2, 256]), tmp.take([2, 256])
        loads.append((w_x[:, 0:256], a["L1_gnn_W1"]))
        for j, name in enumerate(("L1_gnn_att_src1", "L1_gnn_att_dst1")):
            loads.append((att[:, j, :], line(a[name].rearrange("h d -> (h d)")).partition_broadcast(P)))
    elif i == 1:
        W.take([264])
        w2x = W.take([2, 130])
        bcast(W.take([256]), "L1_gnn_bias1")
        att, prod = tmp.take([2, D]), tmp.take([2, 2, D])
        loads.append((w2x[:, :, 0:D], a["L1_gnn_W2"].rearrange("(k p) d -> p k d", p=P)))
        for j, name in enumerate(("L1_gnn_att_src2", "L1_gnn_att_dst2")):
            loads.append((att[:, j, :], a[name].partition_broadcast(P)))
    elif i == 2:
        bcast(W.take([D]), "L1_gnn_bias2")
    else:
        w_l, w_r = W.take([D]), W.take([D])
        raw = tmp.take([2, D])
        names = ("L2_gnn_W1l", "L2_gnn_W1r", "L2_gnn_b1l") if i == 3 else ("L2_gnn_W2l", "L2_gnn_W2r", "L2_gnn_b2l")
        loads += [(raw[:, 0, :], a[names[0]]), (raw[:, 1, :], a[names[1]])]
        bcast(W.take([D]), names[2])
        if i == 4:
            loads += [(L.wq, a["L3_gnn_Wq_w"]), (L.wk, a["L3_gnn_Wk_w"]),
                      (L.wo, a["L3_gnn_Wo_w"].rearrange("(j p) d -> p j d", p=P))]
            bcast(L.bqk[:, 0:256], "L3_gnn_Wq_b")
            bcast(L.bqk[:, 256:512], "L3_gnn_Wk_b")
            bcast(L.bo, "L3_gnn_Wo_b")

    with nc.Block() as block:
        @block.sync
        def _(sp):
            for to, of in loads:
                sp.dma_start(to, of).then_inc(m.loaded.sem, 16)
            sp.wait_ge(m.loaded.sem, m.loaded.past + 16 * len(loads))

        @block.vector
        def _(v):
            v.wait_ge(m.loaded.sem, m.loaded.past + 16 * len(loads))
            if i == 0:
                v.tensor_tensor(prod, att, w_x[:, 0:256].unsqueeze(1).to_broadcast([P, 2, 256]), ALU.mult)
                v.drain()
                v.tensor_reduce(w_x[:, 256:264], prod.rearrange("p j (h c) -> p (j h) c", c=64), AX, ALU.add)
            elif i == 1:
                for k in range(2):
                    v.tensor_tensor(prod[:, k], att, w2x[:, k:k + 1, 0:D].to_broadcast([P, 2, D]), ALU.mult)
                v.drain()
                v.tensor_reduce(w2x[:, :, D:D + 2], prod, AX, ALU.add)
            elif i >= 3:
                v.wait_ge(m.pe_to_vec.sem, m.pe_to_vec.past + 1)
                v.tensor_copy(w_l, m.pa[:, 0:P])
                v.tensor_copy(w_r, m.pa[:, P:2 * P])
            v.drain()

        @block.tensor
        def _(pe):
            if i >= 3:
                pe.wait_ge(m.loaded.sem, m.loaded.past + 16 * len(loads))
                pe.transpose(m.pa[:, 0:P], raw[:, 0, :], m.ident)
                pe.transpose(m.pa[:, P:2 * P], raw[:, 1, :], m.ident).then_inc(m.pe_to_vec.sem, 1)

    m.loaded.ended(16 * len(loads))
    if i >= 3:
        m.pe_to_vec.ended(1)


def gnn_program(nc, a, out):
    m = allocate(nc)
    setup(nc, m, a["src"], a["dst"])
    table_init(nc, m, a)
    for i in range(9):
        if i < 3:
            edge_weights(nc, m, i)
        if i < 5:
            prepare(nc, m, i, a)
        edge_pass(nc, m, i, a, out)


def kernel(**inputs):
    import concourse.bacc as bacc
    from concourse.bass_utils import run_bass_kernel_spmd

    nc = bacc.Bacc("TRN2", target_bir_lowering=False, num_devices=1)
    arrays, a = {}, {}
    for name, value in inputs.items():
        value = np.ascontiguousarray(value)
        arrays[f"in_{name}"] = value
        a[name] = nc.dram_tensor(f"in_{name}", value.shape, mybir.dt.from_np(value.dtype), kind="ExternalInput").ap()
    out = nc.dram_tensor("out", (N, D), F32, kind="ExternalOutput").ap()
    gnn_program(nc, a, out)
    return run_bass_kernel_spmd(nc, [arrays], core_ids=[0]).results[0]["out"]
```
